# Optimizing a Trainium2 kernel written in Bass

```python
import numpy as np
import jax
import jax.numpy as jnp

def _softmax(x, axis=-1):
    return jax.nn.softmax(x, axis=axis)

def _gelu(x):
    return jax.nn.gelu(x, approximate=True)

def _silu(x):
    return jax.nn.silu(x)

def _sigmoid(x):
    return jax.nn.sigmoid(x)

def _layernorm(x, axis=-1, eps=1e-05):
    m = jnp.mean(x, axis=axis, keepdims=True)
    v = jnp.var(x, axis=axis, keepdims=True)
    return (x - m) / jnp.sqrt(v + eps)

def _scatter_add(tgt, idx, src, axis=0):
    return tgt.at[idx].add(src)

def _segment_sum(src, seg, n):
    return jax.ops.segment_sum(src, seg, n)
kernel_name = 'mk_hybrid_d1_jaxref_r8_0c0990'

def setup_inputs(seed: int=0):
    np.random.seed(seed)
    _w = jnp.asarray

    def _L0_attn_a_setup():
        import jax, jax.numpy as jnp
        import numpy as np
        DIM = 128
        H = 16
        KV = 2
        D = DIM // H
        W = 32
        HW = W // 2
        key = jax.random.key(seed)
        ks = jax.random.split(key, 9)
        B, S = (2, 512)
        n = lambda k, shp, sc=1.0: jax.random.normal(k, shp, jnp.float32) * sc
        return {'x': n(ks[0], (B, S, DIM)), 'Wq': n(ks[1], (DIM, H * D), 0.02), 'bq': n(ks[2], (H * D,), 0.02), 'Wk': n(ks[3], (DIM, KV * D), 0.02), 'bk': n(ks[4], (KV * D,), 0.02), 'Wv': n(ks[5], (DIM, KV * D), 0.02), 'bv': n(ks[6], (KV * D,), 0.02), 'Wo': n(ks[7], (DIM, DIM), 0.02), 'bo': n(ks[8], (DIM,), 0.02)}
    _L0_attn_a_in = _L0_attn_a_setup()

    def _L0_attn_b_setup():
        import jax, jax.numpy as jnp
        import numpy as np
        B, T, C = (4, 512, 128)
        H = 16
        D = C // H
        EPS = 1e-06

        def _phi(x):
            return jax.nn.elu(x) + 1.0
        key = jax.random.key(seed)
        k1, k2, k3 = jax.random.split(key, 3)
        x = jax.random.normal(k1, (B, T, C), dtype=jnp.float32)
        Wqkv = jax.random.normal(k2, (3 * C, C), dtype=jnp.float32) * (1.0 / np.sqrt(C))
        Wproj = jax.random.normal(k3, (C, C), dtype=jnp.float32) * (1.0 / np.sqrt(C))
        bproj = jnp.zeros((C,), dtype=jnp.float32)
        return {'x': x, 'Wqkv': Wqkv, 'Wproj': Wproj, 'bproj': bproj}
    _L0_attn_b_in = _L0_attn_b_setup()

    def _L0_ffn_setup():
        import jax, jax.numpy as jnp
        import numpy as np
        D_MODEL = 128
        EXPANSION = 4
        D_HIDDEN = D_MODEL * EXPANSION
        NUM_STAGES = int(np.log2(D_HIDDEN))

        def butterfly(y, weights, dim):
            lead = y.shape[:-1]
            for stage in range(weights.shape[0]):
                s = 2 ** stage
                nb = dim // (2 * s)
                yr = y.reshape(*lead, nb, 2, s)
                a = yr[..., 0, :]
                b = yr[..., 1, :]
                w = weights[stage].reshape(nb, s, 2, 2)
                na = w[..., 0, 0] * a + w[..., 0, 1] * b
                nb2 = w[..., 1, 0] * a + w[..., 1, 1] * b
                y = jnp.stack([na, nb2], axis=-2).reshape(*lead, dim)
            return y
        key = jax.random.key(seed)
        ks = jax.random.split(key, 6)
        B, S = (4, 256)
        x = jax.random.normal(ks[0], (B, S, D_MODEL), jnp.float32)
        W_exp = jax.random.normal(ks[1], (D_MODEL, D_HIDDEN), jnp.float32) * 0.02
        b_exp = jnp.zeros((D_HIDDEN,), jnp.float32)
        up_weights = jax.random.normal(ks[2], (NUM_STAGES, D_HIDDEN // 2, 2, 2), jnp.float32) * 0.02
        up_bias = jnp.zeros((D_HIDDEN,), jnp.float32)
        down_weights = jax.random.normal(ks[3], (NUM_STAGES, D_HIDDEN // 2, 2, 2), jnp.float32) * 0.02
        W_con = jax.random.normal(ks[4], (D_HIDDEN, D_MODEL), jnp.float32) * 0.02
        b_con = jnp.zeros((D_MODEL,), jnp.float32)
        down_bias = jnp.zeros((D_MODEL,), jnp.float32)
        return dict(x=x, W_exp=W_exp, b_exp=b_exp, up_weights=up_weights, up_bias=up_bias, down_weights=down_weights, W_con=W_con, b_con=b_con, down_bias=down_bias)
    _L0_ffn_in = _L0_ffn_setup()
    _d = {'L0_attn_a_x': _L0_attn_a_in['x'], 'L0_attn_a_Wq': _L0_attn_a_in['Wq'], 'L0_attn_a_bq': _L0_attn_a_in['bq'], 'L0_attn_a_Wk': _L0_attn_a_in['Wk'], 'L0_attn_a_bk': _L0_attn_a_in['bk'], 'L0_attn_a_Wv': _L0_attn_a_in['Wv'], 'L0_attn_a_bv': _L0_attn_a_in['bv'], 'L0_attn_a_Wo': _L0_attn_a_in['Wo'], 'L0_attn_a_bo': _L0_attn_a_in['bo'], 'L0_attn_b_Wqkv': _L0_attn_b_in['Wqkv'], 'L0_attn_b_Wproj': _L0_attn_b_in['Wproj'], 'L0_attn_b_bproj': _L0_attn_b_in['bproj'], 'L0_ffn_W_exp': _L0_ffn_in['W_exp'], 'L0_ffn_b_exp': _L0_ffn_in['b_exp'], 'L0_ffn_up_weights': _L0_ffn_in['up_weights'], 'L0_ffn_up_bias': _L0_ffn_in['up_bias'], 'L0_ffn_down_weights': _L0_ffn_in['down_weights'], 'L0_ffn_W_con': _L0_ffn_in['W_con'], 'L0_ffn_b_con': _L0_ffn_in['b_con'], 'L0_ffn_down_bias': _L0_ffn_in['down_bias']}
    _x0 = _d['L0_attn_a_x']
    _d['L0_attn_a_x'] = jax.random.normal(jax.random.fold_in(jax.random.key(seed), 1), (32, 256, 128), dtype=_x0.dtype)
    del _x0
    return _d

def reference(L0_attn_a_x, L0_attn_a_Wq, L0_attn_a_bq, L0_attn_a_Wk, L0_attn_a_bk, L0_attn_a_Wv, L0_attn_a_bv, L0_attn_a_Wo, L0_attn_a_bo, L0_attn_b_Wqkv, L0_attn_b_Wproj, L0_attn_b_bproj, L0_ffn_W_exp, L0_ffn_b_exp, L0_ffn_up_weights, L0_ffn_up_bias, L0_ffn_down_weights, L0_ffn_W_con, L0_ffn_b_con, L0_ffn_down_bias):

    def _L0_attn_a_ref(x, Wq, bq, Wk, bk, Wv, bv, Wo, bo):
        import jax, jax.numpy as jnp
        import numpy as np
        DIM = 128
        H = 16
        KV = 2
        D = DIM // H
        W = 32
        HW = W // 2
        B, S, _ = x.shape
        q = (x @ Wq + bq).reshape(B, S, H, D).transpose(0, 2, 1, 3)
        k = (x @ Wk + bk).reshape(B, S, KV, D).transpose(0, 2, 1, 3)
        v = (x @ Wv + bv).reshape(B, S, KV, D).transpose(0, 2, 1, 3)
        rep = H // KV
        k = jnp.repeat(k, rep, axis=1)
        v = jnp.repeat(v, rep, axis=1)
        pad = ((0, 0), (0, 0), (HW, HW), (0, 0))
        pk = jnp.pad(k, pad)
        pv = jnp.pad(v, pad)
        nblk = S // W
        pk = pk.reshape(B, H, nblk + 1, W, D)
        pv = pv.reshape(B, H, nblk + 1, W, D)
        kb = jnp.concatenate([pk[:, :, :-1], pk[:, :, 1:]], axis=3)
        vb = jnp.concatenate([pv[:, :, :-1], pv[:, :, 1:]], axis=3)
        qb = q.reshape(B, H, nblk, W, D)
        scores = jnp.einsum('bhntd,bhnud->bhntu', qb, kb)
        t = jnp.arange(W)[:, None]
        u = jnp.arange(2 * W)[None, :]
        win_mask = (u >= t) & (u < t + W)
        scores = jnp.where(win_mask, scores, -jnp.inf)
        probs = jax.nn.softmax(scores, axis=-1)
        out = jnp.einsum('bhntu,bhnud->bhntd', probs, vb)
        out = out.reshape(B, H, S, D).transpose(0, 2, 1, 3).reshape(B, S, H * D)
        return out @ Wo + bo

    def _L0_attn_b_ref(x, Wqkv, Wproj, bproj):
        import jax, jax.numpy as jnp
        import numpy as np
        B, T, C = (4, 512, 128)
        H = 16
        D = C // H
        EPS = 1e-06

        def _phi(x):
            return jax.nn.elu(x) + 1.0
        b, t, c = x.shape
        qkv = jnp.einsum('btc,ec->bte', x, Wqkv)
        qkv = qkv.reshape(b, t, 3, H, D)
        q, k, v = (qkv[:, :, 0], qkv[:, :, 1], qkv[:, :, 2])
        q = _phi(q)
        k = _phi(k)
        kv = jnp.einsum('bnhd,bnhm->bhdm', k, v)
        k_sum = k.sum(axis=1)
        out = jnp.einsum('bnhd,bhdm->bnhm', q, kv)
        normalizer = jnp.einsum('bnhd,bhd->bnh', q, k_sum) + EPS
        out = out / normalizer[..., None]
        out = out.reshape(b, t, c)
        out = jnp.einsum('btc,oc->bto', out, Wproj) + bproj
        return out

    def _L0_ffn_ref(x, W_exp, b_exp, up_weights, up_bias, down_weights, W_con, b_con, down_bias):
        import jax, jax.numpy as jnp
        import numpy as np
        D_MODEL = 128
        EXPANSION = 4
        D_HIDDEN = D_MODEL * EXPANSION
        NUM_STAGES = int(np.log2(D_HIDDEN))

        def butterfly(y, weights, dim):
            lead = y.shape[:-1]
            for stage in range(weights.shape[0]):
                s = 2 ** stage
                nb = dim // (2 * s)
                yr = y.reshape(*lead, nb, 2, s)
                a = yr[..., 0, :]
                b = yr[..., 1, :]
                w = weights[stage].reshape(nb, s, 2, 2)
                na = w[..., 0, 0] * a + w[..., 0, 1] * b
                nb2 = w[..., 1, 0] * a + w[..., 1, 1] * b
                y = jnp.stack([na, nb2], axis=-2).reshape(*lead, dim)
            return y
        h = jnp.einsum('bsd,dh->bsh', x, W_exp) + b_exp
        h = butterfly(h, up_weights, D_HIDDEN)
        h = jax.nn.gelu(h + up_bias, approximate=False)
        h = butterfly(h, down_weights, D_HIDDEN)
        y = jnp.einsum('bsh,hd->bsd', h, W_con) + b_con
        return y + down_bias
    x = L0_attn_a_x
    x = x + _L0_attn_a_ref(_layernorm(x, axis=-1), L0_attn_a_Wq, L0_attn_a_bq, L0_attn_a_Wk, L0_attn_a_bk, L0_attn_a_Wv, L0_attn_a_bv, L0_attn_a_Wo, L0_attn_a_bo)
    x = x + _L0_ffn_ref(_layernorm(x, axis=-1), L0_ffn_W_exp, L0_ffn_b_exp, L0_ffn_up_weights, L0_ffn_up_bias, L0_ffn_down_weights, L0_ffn_W_con, L0_ffn_b_con, L0_ffn_down_bias)
    x = x + _L0_attn_b_ref(_layernorm(x, axis=-1), L0_attn_b_Wqkv, L0_attn_b_Wproj, L0_attn_b_bproj)
    x = x + _L0_ffn_ref(_layernorm(x, axis=-1), L0_ffn_W_exp, L0_ffn_b_exp, L0_ffn_up_weights, L0_ffn_up_bias, L0_ffn_down_weights, L0_ffn_W_con, L0_ffn_b_con, L0_ffn_down_bias)
    return x

_drawn_inputs = setup_inputs


def setup_inputs(seed=0):
    import zlib

    import numpy as np

    out = dict(_drawn_inputs(seed))
    spreads = {'L0_attn_b_bproj': (0.0, 0.1),
     'L0_ffn_b_exp': (0.0, 0.1),
     'L0_ffn_up_bias': (0.0, 0.1),
     'L0_ffn_b_con': (0.0, 0.1),
     'L0_ffn_down_bias': (0.0, 0.1)}
    factors = {'L0_attn_a_Wq': 8.0,
     'L0_attn_a_bq': 8.0,
     'L0_attn_a_Wk': 8.0,
     'L0_attn_a_bk': 64.0,
     'L0_attn_a_Wv': 5.986,
     'L0_attn_a_bv': 8.0,
     'L0_attn_a_Wo': 5.082,
     'L0_attn_a_bo': 4.103}
    for name, (base, spread) in spreads.items():
        noise = np.random.default_rng([zlib.crc32(name.encode()), seed]).standard_normal(out[name].shape)
        drawn = base * np.exp(spread * noise) if base else spread * noise
        out[name] = jnp.asarray(drawn.astype(out[name].dtype))
    for name, factor in factors.items():
        out[name] = (out[name] * factor).astype(out[name].dtype)
    return out
```

```python
from contextlib import ExitStack

import numpy as np

import concourse.bass as bass
from concourse import mybir

F32 = mybir.dt.float32
BF16 = mybir.dt.bfloat16
ALU = mybir.AluOpType
ACT = mybir.ActivationFunctionType
AX_X = mybir.AxisListType.X

BATCH, SEQ, DIM = 32, 256, 128
HEADS, KV, HD = 16, 2, 8
HPK = HEADS // KV
WIN = 32
SPAN = 2 * WIN
PAD = WIN // 2
P = 128
TSPAN = P + 2 * PAD
TILES = 4
TOK = TILES * P
GB = TOK // SEQ
TPB = SEQ // P
NG = BATCH * SEQ // TOK
HID = 512
CH = HID // P
STAGES = HID.bit_length() - 1
KVW = DIM + HEADS
LN_EPS = 1e-5
LIN_EPS = 1e-6
MASKED = -1e30
SLOTS = 4

LAG = {"P": 0, "W": 1, "F": 2, "L": 3, "G": 4}
TURNS = NG + max(LAG.values())
FULL = range(max(LAG.values()) + 1, NG)


def active(turn, stage):
    return not isinstance(turn, int) or 0 <= turn - LAG[stage] < NG


def value(eng, v):
    return v if isinstance(v, int) else eng.to_reg(v)


class Count:

    def __init__(self, sem, events, unit=1):
        self.sem, self.events, self.unit = sem, events, unit

    def after(self, turn, event):
        at = self.events.index(event)
        groups = [turn - LAG[e[0]] + (1 if k <= at else 0) for k, e in enumerate(self.events)]
        if isinstance(turn, int):
            return self.unit * sum(min(max(g, 0), NG) for g in groups)
        lag = sum(LAG[e[0]] - (1 if k <= at else 0) for k, e in enumerate(self.events))
        return turn * (self.unit * len(self.events)) - self.unit * lag


PRODUCTS = [
    ("W.S0", "S"), ("L.xT", "0"), ("L.q", "1"), ("L.k0", "2"), ("L.k1", "3"), ("W.S1", "S"),
    ("W.T0", "T"), ("L.kv", "0"), ("W.V", "1"), ("W.S2", "S"), ("W.T1", "T"), ("W.PV0", "2"),
    ("L.out0", "3"), ("L.out1", "0"), ("W.S3", "S"), ("W.PV1", "1"), ("W.T2", "T"), ("F.xT", "2"),
    ("F.up0", "3"), ("F.up1", "0"), ("F.up2", "1"), ("F.up3", "2"), ("P.xT", "3"), ("P.kv", "0"),
    ("P.q", "1"), ("W.T3", "T"), ("W.PV2", "2"), ("G.xT", "3"), ("G.up0", "0"), ("G.up1", "1"),
    ("G.up2", "2"), ("G.up3", "3"), ("W.PV3", "0"), ("F.down", "1"), ("W.oT", "2"), ("L.oT", "3"),
    ("W.proj", "0"), ("L.proj", "1"), ("G.down", "2"),
]
BANK = dict(PRODUCTS)


def window_and_linear_attention_with_butterfly_ffn(
    nc, x, wq, bq, wk, bk, wv, bv, wo, bo, wqkv_t, wproj_t, bproj, w_exp, b_exp, up_w, up_b,
    down_w, w_con_t, b_con, down_b, ident_c, kvmask_c, band_c, vones_c, out,
):
    with ExitStack() as ctx:
        def sb(name, shape, dt=F32):
            return ctx.enter_context(nc.sbuf_tensor(name, shape, dt))

        def sem(name):
            return ctx.enter_context(nc.semaphore(name))

        ident = sb("ident", [P, P])
        identb = sb("identb", [P, P], BF16)
        kvmask = sb("kvmask", [P, KVW])
        band = sb("band", [P, SPAN])
        bandb = sb("bandb", [P, HPK, SPAN], BF16)
        half = sb("half", [P, TILES])
        wq_s = sb("wq_s", [P, P])
        wkv_s = sb("wkv_s", [P, 2 * KV * HD])
        wo_s = sb("wo_s", [P, P])
        wl_s = sb("wl_s", [P, 3 * P])
        wp_s = sb("wp_s", [P, P])
        bq_s = sb("bq_s", [P, 1])
        bkv_s = sb("bkv_s", [2 * KV * HD, 1])
        bo_s = sb("bo_s", [P, P])
        bproj_s = sb("bproj_s", [P, P])
        bcon_s = sb("bcon_s", [P, P])
        bdown_s = sb("bdown_s", [P, P])
        bffn_s = sb("bffn_s", [P, P])
        up_s = sb("up_s", [P, SLOTS, 4 * HID // 2])
        down_s = sb("down_s", [P, SLOTS, 4 * HID // 2])
        w1 = sb("w1", [P, HID])
        w1b = sb("w1b", [P, HID])
        w2t = sb("w2t", [P, HID])
        w2tb = sb("w2tb", [P, HID])
        w2 = sb("w2", [P, CH, P])
        b1row = sb("b1row", [1, HID])
        b1rowb = sb("b1rowb", [1, HID])
        upb_row = sb("upb_row", [1, HID])
        b1 = sb("b1", [P, CH])
        prod0 = sb("prod0", [P, HID])
        prod1 = sb("prod1", [P, HID])
        row0 = sb("row0", [1, HID])
        row1 = sb("row1", [1, HID])
        dprod0 = sb("dprod0", [P, HID])
        dprod1 = sb("dprod1", [P, HID])

        xs = {s: sb(f"x_{s}", [P, TILES, P]) for s in "PWFLG"}
        xn = {s: sb(f"xn_{s}", [P, TILES, P]) for s in "PWFL"}
        xb = {s: sb(f"xb_{s}", [P, TILES, P]) for s in "PWFL"}
        stats = {s: sb(f"stats_{s}", [P, TILES, 6]) for s in "PWFL"}
        mv = {s: sb(f"mv_{s}", [P, TILES, 2]) for s in "PWFL"}
        rv = {s: sb(f"rv_{s}", [P, TILES]) for s in "PWFL"}
        nm = {s: sb(f"nm_{s}", [P, TILES]) for s in "PWFL"}
        rstd = {s: sb(f"rstd_{s}", [P, TILES]) for s in "PWFL"}
        nmr = {s: sb(f"nmr_{s}", [P, TILES]) for s in "PWFL"}
        x_t = {s: sb(f"xT_{s}", [P, TOK]) for s in "PFLG"}
        q_t = sb("q_t", [P, TOK])
        kv_t = sb("kv_t", [2 * KV * HD, TILES, TSPAN])
        kx = sb("kx", [P, HEADS, TILES * TSPAN])
        vx_t = sb("vx_t", [P, TILES, KV * SPAN])
        vx = sb("vx", [P, TILES, 4, 32])
        rowmax = sb("rowmax", [P, TILES, HEADS])
        probs = sb("probs", [P, 2, HPK, KV, SPAN])
        probs_t = sb("probs_t", [P, 2, HPK, P])
        o_raw = sb("o_raw", [P, 2, HPK, 32])
        recip = sb("recip", [P, 2, KV, HPK])
        o_w = sb("o_w", [P, TILES, P])
        o_wt = sb("o_wt", [P, TOK])
        hid = {s: sb(f"hid_{s}", [P, CH, TOK]) for s in "FG"}
        neg_q = sb("neg_q", [P, TOK])
        phi_q = sb("phi_q", [P, TOK])
        neg_k = sb("neg_k", [P, 2, 2, P])
        phi_k = sb("phi_k", [P, TILES, P])
        v_ext = sb("v_ext", [P, TILES, KVW])
        kvs = sb("kvs", [P, GB, KVW])
        norm = sb("norm", [P, 2, 2, HEADS])
        rnorm = sb("rnorm", [P, 2, 2, HEADS])
        o_l = sb("o_l", [P, TILES, P])
        o_lt = sb("o_lt", [P, TOK])

        ps_s = ctx.enter_context(nc.psum_tensor("ps_s", [P, 2, 512], F32))
        ps_t = ctx.enter_context(nc.psum_tensor("ps_t", [P, HPK, P], F32))
        ring = [ctx.enter_context(nc.psum_tensor(f"ring{i}", [P, 512], F32)) for i in range(4)]

        def bank(name):
            return ring[int(BANK[name])]

        consts_in = sem("consts_in")
        weights_in = sem("weights_in")
        up_in = [sem(f"up_in{n}") for n in range(STAGES)]
        down_in = [sem(f"down_in{n}") for n in range(STAGES)]
        cleared = sem("cleared")
        half_set = sem("half_set")
        consts_made = sem("consts_made")
        up_step = sem("up_step")
        bias_step = sem("bias_step")
        down_step = sem("down_step")
        prep_product = sem("prep_product")
        b1_made = sem("b1_made")
        w2_made = sem("w2_made")
        bffn_made = sem("bffn_made")

        product = Count(sem("product"), [n for n, _ in PRODUCTS])
        drained = {b: Count(sem(f"drained_{b}"), [n for n, k in PRODUCTS if k == b]) for b in "ST0123"}
        vec = Count(sem("vector_result"), [
            "W.max0", "P.bn", "P.mv", "W.max1", "W.max2", "W.rs0", "W.o0", "L.nrm0", "L.rn0", "L.nrm1", "L.rn1",
            "W.max3", "W.rs1", "W.o1", "W.rs2", "W.o2", "W.rs3", "W.o3", "F.bn", "F.mv",
            "W.bn", "W.mv", "L.bn", "L.mv"])
        probs_ready = Count(sem("probs_ready"), ["W.0", "W.1", "W.2", "W.3"])
        negated = Count(sem("negated"), ["L.q", "L.k0", "L.k1"])
        phi_exp = Count(sem("phi_exp"), ["L.q", "L.k0", "L.k1"])
        pool_step = Count(sem("pool_step"), [f"{s}.{e}" for s in "PFLW" for e in ("rv", "rstd", "nm", "nmr")])
        normed = Count(sem("normed"), [f"{s}.xn" for s in "PFLW"])
        biased = Count(sem("biased"), ["P.xb", "F.xb", "L.xb", "W.xb"])
        x_in = Count(sem("x_in"), ["P.x"], 16)
        kx_in = Count(sem("kx_in"), ["P.kx"], 16 * HEADS)
        v_in = Count(sem("v_in"), ["P.v"], 16 * 4 * KV)
        y_out = Count(sem("y_out"), ["G.y"], 16)

        x_v = x.rearrange("b (j p) d -> (b j) p d", p=P).rearrange("(g j) p d -> g p j d", j=TILES)
        y_v = out.rearrange("b (j p) d -> (b j) p d", p=P).rearrange("(g j) p d -> g p j d", j=TILES)

        def row(ap):
            return ap.rearrange("(a n) -> a n", a=1)

        def column(ap):
            return ap.rearrange("(n a) -> n a", a=1)

        def split(ap, s, rows=P):
            w = 2 ** s
            return ap[0:rows].rearrange("p (o b w) -> p b o w", o=2, w=w)

        def paired(ap, s, rows=P):
            w = 2 ** s
            return ap[0:rows].rearrange("p (b o w) -> p b o w", o=2, w=w)

        def products(eng, weights, s, src, to0, to1, step, rows=P):
            w = 2 ** s
            coef = weights[0:rows].rearrange("p (o i k) -> p o i k", o=2, i=2)
            for i, to in ((0, to0), (1, to1)):
                xin = src[0:rows].rearrange("p (b i w) -> p i b w", i=2, w=w)[:, i]
                for o in range(2):
                    last = eng.tensor_tensor(
                        to[0:rows, o * HID // 2:(o + 1) * HID // 2].rearrange("p (b w) -> p b w", w=w),
                        coef[:, o, i].rearrange("p (b w) -> p b w", w=w), xin, ALU.mult)
                last.then_inc(step, 1)

        block = ctx.enter_context(nc.Block())

        @block.sync
        def _(sp):
            consts = [(ident, ident_c), (kvmask, kvmask_c), (band, band_c)]
            for dst, src in consts:
                sp.dma_start(dst[:], src).then_inc(consts_in, 16)
            sp.dma_start(vx_t[:], vones_c.rearrange("p (a n) -> p a n", a=1).to_broadcast([P, TILES, P])
                         ).then_inc(consts_in, 16)
            weights = [
                (wq_s[:], wq), (wkv_s[:, 0:KV * HD], wk), (wkv_s[:, KV * HD:], wv), (bq_s[:], column(bq)),
                (bkv_s[0:KV * HD, :], column(bk)), (bkv_s[KV * HD:, :], column(bv)), (wo_s[:], wo),
                (bo_s[:], row(bo).to_broadcast([P, P])), (wl_s[:], wqkv_t), (wp_s[:], wproj_t),
                (bproj_s[:], row(bproj).to_broadcast([P, P])), (bcon_s[:], row(b_con).to_broadcast([P, P])),
                (bdown_s[:], row(down_b).to_broadcast([P, P])), (w1[:], w_exp), (w2t[:], w_con_t),
                (b1row[:], row(b_exp)), (upb_row[:], row(up_b)),
            ]
            assert len(weights) == N_WEIGHTS

            def turn(t):
                if active(t, "P"):
                    seen = value(sp, normed.after(t - 1, "P.xn"))
                    sp.wait_ge(consts_in, 16 * 4)
                    sp.wait_ge(normed.sem, seen)
                    seen = value(sp, biased.after(t - 1, "P.xb"))
                    sp.wait_ge(consts_in, 16 * 4)
                    sp.wait_ge(biased.sem, seen)
                    sp.dma_start(xs["P"][:], x_v[t]).then_inc(x_in.sem, 16)
                if isinstance(t, int) and t == 0:
                    for dst, src in weights:
                        sp.dma_start(dst, src).then_inc(weights_in, 16)
                    for n in range(SLOTS):
                        butterfly_weights(n)
                if active(t, "P"):
                    seen = value(sp, drained[BANK["P.kv"]].after(t, "P.kv"))
                    sp.wait_ge(consts_in, 16 * 4)
                    sp.wait_ge(drained[BANK["P.kv"]].sem, seen)
                    sp.wait_ge(cleared, N_CLEARED)
                    seen = value(sp, product.after(t, "W.V"))
                    sp.wait_ge(consts_in, 16 * 4)
                    sp.wait_ge(product.sem, seen)
                    sp.wait_ge(consts_in, 16 * 4)
                    for c in range(4):
                        for kv in range(KV):
                            r = KV * HD + kv * HD
                            sp.dma_start(vx_t[32 * c + kv * HD:32 * c + (kv + 1) * HD, :, kv * SPAN:(kv + 1) * SPAN],
                                         kv_t[r:r + HD, :, 32 * c:32 * c + SPAN]).then_inc(v_in.sem, 16)
                    seen = value(sp, product.after(t, "W.S3"))
                    sp.wait_ge(consts_in, 16 * 4)
                    sp.wait_ge(product.sem, seen)
                    for h in range(HEADS):
                        kv = h // HPK
                        sp.dma_start(kx[h * HD:(h + 1) * HD, h],
                                     kv_t[kv * HD:(kv + 1) * HD].rearrange("d j n -> d (j n)")).then_inc(kx_in.sem, 16)
                if isinstance(t, int) and t == 0:
                    for n in range(SLOTS, STAGES):
                        sp.wait_ge(bias_step, 3 * (n - SLOTS) + 2)
                        sp.wait_ge(down_step, 3 * (n - SLOTS) + 2)
                        butterfly_weights(n)

                if active(t, "G"):
                    seen = value(sp, drained[BANK["G.down"]].after(t, "G.down"))
                    sp.wait_ge(consts_in, 16 * 4)
                    sp.wait_ge(drained[BANK["G.down"]].sem, seen)
                    sp.dma_start(y_v[t - LAG["G"]], xs["G"][:]).then_inc(y_out.sem, 16)

            def butterfly_weights(n):
                m = STAGES - 1 - n
                sp.dma_start(up_s[:, n % SLOTS], up_w[n:n + 1].to_broadcast([P, 2 * HID])).then_inc(up_in[n], 16)
                sp.dma_start(down_s[:, n % SLOTS], down_w[m:m + 1].to_broadcast([P, 2 * HID])
                             ).then_inc(down_in[n], 16)

            for t in range(FULL[0]):
                turn(t)
            with sp.Fori(FULL[0], FULL[-1] + 1) as t:
                turn(t)
            for t in range(FULL[-1] + 1, TURNS):
                turn(t)
            sp.wait_ge(y_out.sem, 16 * NG)

        @block.gpsimd
        def _(pool):
            nc.gpsimd.memset(half[:], -0.5).then_inc(half_set, 1)
            nc.gpsimd.memset(kv_t[:], 0.0).then_inc(cleared, 1)
            nc.gpsimd.memset(v_ext[:], 1.0).then_inc(cleared, 1)
            nc.gpsimd.memset(kx[:], 0.0).then_inc(cleared, 1)

            def normalise(t, s, freed_t, freed):
                seen = value(pool, vec.after(t, f"{s}.mv"))
                pool.wait_ge(half_set, 1)
                pool.wait_ge(vec.sem, seen)
                nc.gpsimd.tensor_scalar(rv[s][:], mv[s][:, :, 1], LN_EPS, None, ALU.add
                                        ).then_inc(pool_step.sem, 1)
                pool.wait_ge(pool_step.sem, pool_step.after(t, f"{s}.rv"))
                nc.gpsimd.tensor_tensor(rstd[s][:], rv[s][:], half[:], ALU.pow).then_inc(pool_step.sem, 1)
                nc.gpsimd.tensor_scalar(nm[s][:], mv[s][:, :, 0], -1.0, None, ALU.mult
                                        ).then_inc(pool_step.sem, 1)
                pool.wait_ge(pool_step.sem, pool_step.after(t, f"{s}.nm"))
                nc.gpsimd.tensor_tensor(nmr[s][:], nm[s][:], rstd[s][:], ALU.mult).then_inc(pool_step.sem, 1)
                seen, read = value(pool, pool_step.after(t, f"{s}.nmr")), value(pool, product.after(freed_t, freed))
                pool.wait_ge(half_set, 1)
                pool.wait_ge(pool_step.sem, seen)
                pool.wait_ge(product.sem, read)
                for j in range(TILES):
                    last = nc.gpsimd.tensor_scalar(xn[s][:, j], xs[s][:, j], rstd[s][:, j:j + 1],
                                                   nmr[s][:, j:j + 1], ALU.mult, ALU.add)
                last.then_inc(normed.sem, 1)

            def add_bias(t, s, bias, freed):
                pool.wait_ge(drained[BANK[freed]].sem, drained[BANK[freed]].after(t, freed))
                nc.gpsimd.tensor_tensor(xb[s][:], xs[s][:], bias[:].rearrange("p (a n) -> p a n", a=1)
                                        .to_broadcast([P, TILES, P]), ALU.add).then_inc(biased.sem, 1)

            def butterfly_down():
                src, dst = w2t, w2tb
                for n, s in enumerate(reversed(range(STAGES))):
                    pool.wait_ge(down_in[n], 16)
                    pool.wait_ge(down_step, 3 * n)
                    products(nc.gpsimd, down_s[:, n % SLOTS], s, src, dprod0, dprod1, down_step)
                    pool.wait_ge(down_step, 3 * n + 2)
                    nc.gpsimd.tensor_tensor(paired(dst, s), split(dprod0, s), split(dprod1, s), ALU.add
                                            ).then_inc(down_step, 1)
                    src, dst = dst, src

            def turn(t):
                if active(t, "P"):
                    normalise(t, "P", t - 1, "P.xT")
                if isinstance(t, int) and t == 0:
                    pool.wait_ge(weights_in, 16 * N_WEIGHTS)
                    nc.gpsimd.tensor_tensor(bffn_s[:], bcon_s[:], bdown_s[:], ALU.add).then_inc(bffn_made, 1)
                    add_bias(t, "P", bo_s, "W.proj")
                    butterfly_down()
                    pool.wait_ge(bffn_made, 1)
                if active(t, "F"):
                    normalise(t, "F", t, "L.xT")
                if active(t, "P") and not (isinstance(t, int) and t == 0):
                    add_bias(t, "P", bo_s, "W.proj")
                if active(t, "F"):
                    add_bias(t, "F", bproj_s, "L.proj")
                if active(t, "L"):
                    normalise(t, "L", t, "G.xT")
                    add_bias(t, "L", bffn_s, "G.down")
                if active(t, "W"):
                    normalise(t, "W", t, "F.xT")
                    add_bias(t, "W", bffn_s, "F.down")

            for t in range(FULL[0]):
                turn(t)
            with pool.Fori(FULL[0], FULL[-1] + 1) as t:
                turn(t)
            for t in range(FULL[-1] + 1, TURNS):
                turn(t)

        @block.tensor
        def _(pe):
            def free(t, name):
                own = drained[BANK[name]]
                at = own.events.index(name)
                value = own.after(t, name) - own.unit
                pe.wait_ge(own.sem, value)

            def transposes(t, name, src):
                for j in range(TILES):
                    last = nc.tensor.transpose(bank(name)[:, P * j:P * (j + 1)], src[:, j], ident[:])
                last.then_inc(product.sem, 1)

            def norm_transposed(t, s, made_t, made):
                name = f"{s}.xT"
                pe.wait_ge(normed.sem, normed.after(made_t, made))
                free(t, name)
                transposes(t, name, xn[made[0]])

            def scores(t, j):
                name = f"W.S{j}"
                if j == 0:
                    pe.wait_ge(kx_in.sem, kx_in.after(t - 1, "P.kx"))
                    pe.wait_ge(drained[BANK["P.q"]].sem, drained[BANK["P.q"]].after(t - 1, "P.q"))
                free(t, name)
                for a in range(2):
                    nc.tensor.matmul(ps_s[:, a], identb[:], bandb[:], start=True, stop=False,
                                     skip_group_check=True)
                    for c in range(4):
                        last = nc.tensor.matmul(
                            ps_s[32 * c:32 * c + 32, a], q_t[:, P * j + 32 * c:P * j + 32 * c + 32],
                            kx[:, HPK * a:HPK * (a + 1), TSPAN * j + 32 * c:TSPAN * j + 32 * c + SPAN],
                            start=False, stop=True, skip_group_check=True)
                last.then_inc(product.sem, 1)

            def values_transposed(t):
                pe.wait_ge(v_in.sem, v_in.after(t - 1, "P.v"))
                free(t, "W.V")
                transposes(t, "W.V", vx_t)

            def probs_transposed(t, j):
                name = f"W.T{j}"
                pe.wait_ge(probs_ready.sem, probs_ready.after(t, f"W.{j}"))
                free(t, name)
                for h in range(HPK):
                    last = nc.tensor.transpose(ps_t[:, h], probs[:, j % 2, h].rearrange("p k u -> p (k u)"), ident[:])
                last.then_inc(product.sem, 1)

            def weighted_values(t, j):
                name = f"W.PV{j}"
                if j == 0:
                    pe.wait_ge(drained[BANK["W.V"]].sem, drained[BANK["W.V"]].after(t, "W.V"))
                pe.wait_ge(drained["T"].sem, drained["T"].after(t, f"W.T{j}"))
                free(t, name)
                for c in range(4):
                    last = nc.tensor.matmul(bank(name)[32 * c:32 * c + 32, 0:HPK * 32], vx[:, j, c],
                                            probs_t[:, j % 2, :, 32 * c:32 * c + 32], start=True, stop=True)
                last.then_inc(product.sem, 1)

            def ffn_up(t, s, c):
                name = f"{s}.up{c}"
                if c == 0:
                    pe.wait_ge(drained[BANK[f"{s}.xT"]].sem, drained[BANK[f"{s}.xT"]].after(t, f"{s}.xT"))
                free(t, name)
                nc.tensor.matmul(bank(name)[:], w1b[:, P * c:P * (c + 1)], x_t[s][:], start=True, stop=True
                                 ).then_inc(product.sem, 1)

            def ffn_down(t, s):
                name = f"{s}.down"
                pe.wait_ge(drained[BANK[f"{s}.up{CH - 1}"]].sem, drained[BANK[f"{s}.up{CH - 1}"]].after(t, f"{s}.up{CH - 1}"))
                free(t, name)
                for j in range(TILES):
                    for c in range(CH):
                        last = nc.tensor.matmul(bank(name)[:, P * j:P * (j + 1)], hid[s][:, c, P * j:P * (j + 1)],
                                                w2[:, c], start=(c == 0), stop=(c == CH - 1))
                last.then_inc(product.sem, 1)

            def project(t, name, src, weights):
                free(t, name)
                for j in range(TILES):
                    last = nc.tensor.matmul(bank(name)[:, P * j:P * (j + 1)], src[:, P * j:P * (j + 1)],
                                            weights[:], start=True, stop=True)
                last.then_inc(product.sem, 1)

            def linear_q(t):
                pe.wait_ge(drained[BANK["L.xT"]].sem, drained[BANK["L.xT"]].after(t, "L.xT"))
                free(t, "L.q")
                nc.tensor.matmul(bank("L.q")[:], wl_s[:, 0:P], x_t["L"][:], start=True, stop=True
                                 ).then_inc(product.sem, 1)

            def linear_kv_rows(t, m):
                name = f"L.k{m}"
                free(t, name)
                for i in range(2):
                    j = 2 * m + i
                    last = nc.tensor.matmul(bank(name)[:, 2 * P * i:2 * P * (i + 1)], x_t["L"][:, P * j:P * (j + 1)],
                                            wl_s[:, P:3 * P], start=True, stop=True)
                last.then_inc(product.sem, 1)

            def attention_inputs(t):
                pe.wait_ge(drained[BANK["P.xT"]].sem, drained[BANK["P.xT"]].after(t, "P.xT"))
                free(t, "P.kv")
                nc.tensor.matmul(bank("P.kv")[0:2 * KV * HD, :], wkv_s[:], x_t["P"][:], start=True, stop=True
                                 ).then_inc(product.sem, 1)
                free(t, "P.q")
                nc.tensor.matmul(bank("P.q")[:], wq_s[:], x_t["P"][:], start=True, stop=True
                                 ).then_inc(product.sem, 1)

            def linear_state(t):
                pe.wait_ge(drained[BANK["L.k1"]].sem, drained[BANK["L.k1"]].after(t, "L.k1"))
                pe.wait_ge(cleared, N_CLEARED)
                free(t, "L.kv")
                for b in range(GB):
                    for i in range(TPB):
                        j = TPB * b + i
                        last = nc.tensor.matmul(bank("L.kv")[:, KVW * b:KVW * (b + 1)], phi_k[:, j], v_ext[:, j],
                                                start=(i == 0), stop=(i == TPB - 1))
                last.then_inc(product.sem, 1)

            def linear_out(t, m):
                name = f"L.out{m}"
                if m == 0:
                    pe.wait_ge(drained[BANK["L.q"]].sem, drained[BANK["L.q"]].after(t, "L.q"))
                    pe.wait_ge(drained[BANK["L.kv"]].sem, drained[BANK["L.kv"]].after(t, "L.kv"))
                free(t, name)
                for i in range(2):
                    j = 2 * m + i
                    last = nc.tensor.matmul(bank(name)[:, KVW * i:KVW * (i + 1)], phi_q[:, P * j:P * (j + 1)],
                                            kvs[:, j // TPB], start=True, stop=True)
                last.then_inc(product.sem, 1)

            def turn(t):
                w, f, l, g, p = (active(t, s) for s in "WFLGP")
                if w:
                    scores(t, 0)
                if l:
                    norm_transposed(t, "L", t - 1, "F.xn")
                    linear_q(t)
                    linear_kv_rows(t, 0)
                    linear_kv_rows(t, 1)
                if w:
                    scores(t, 1)
                    probs_transposed(t, 0)
                if l:
                    linear_state(t)
                if w:
                    values_transposed(t)
                    scores(t, 2)
                    probs_transposed(t, 1)
                    weighted_values(t, 0)
                if l:
                    linear_out(t, 0)
                    linear_out(t, 1)
                if w:
                    scores(t, 3)
                    weighted_values(t, 1)
                    probs_transposed(t, 2)
                if f:
                    norm_transposed(t, "F", t - 1, "W.xn")
                    if isinstance(t, int) and t == LAG["F"]:
                        pe.wait_ge(w2_made, 1)
                    for c in range(CH):
                        ffn_up(t, "F", c)
                if p:
                    norm_transposed(t, "P", t, "P.xn")
                    attention_inputs(t)
                if w:
                    probs_transposed(t, 3)
                    weighted_values(t, 2)
                if g:
                    norm_transposed(t, "G", t - 1, "L.xn")
                    for c in range(CH):
                        ffn_up(t, "G", c)
                if w:
                    weighted_values(t, 3)
                if f:
                    ffn_down(t, "F")
                if w:
                    pe.wait_ge(vec.sem, vec.after(t, "W.o3"))
                    free(t, "W.oT")
                    transposes(t, "W.oT", o_w)
                if l:
                    pe.wait_ge(drained[BANK["L.out1"]].sem, drained[BANK["L.out1"]].after(t, "L.out1"))
                    free(t, "L.oT")
                    transposes(t, "L.oT", o_l)
                if w:
                    pe.wait_ge(drained[BANK["W.oT"]].sem, drained[BANK["W.oT"]].after(t, "W.oT"))
                    project(t, "W.proj", o_wt, wo_s)
                if l:
                    pe.wait_ge(drained[BANK["L.oT"]].sem, drained[BANK["L.oT"]].after(t, "L.oT"))
                    project(t, "L.proj", o_lt, wp_s)
                if g:
                    ffn_down(t, "G")

            pe.wait_ge(consts_in, 16 * 4)
            pe.wait_ge(consts_made, 2)
            pe.wait_ge(weights_in, 16 * N_WEIGHTS)
            for t in range(FULL[0]):
                turn(t)
                if t == 0:
                    pe.wait_ge(down_step, 3 * STAGES)
                    for c in range(CH):
                        last = nc.tensor.transpose(ps_t[:, c], w2tb[:, P * c:P * (c + 1)], ident[:])
                    last.then_inc(prep_product, 1)
                    pe.wait_ge(bias_step, 3 * STAGES + 1)
                    for c in range(CH):
                        last = nc.tensor.matmul(ps_t[:, CH, c:c + 1], b1rowb[:, P * c:P * (c + 1)],
                                                ident[0:1, 0:1], start=True, stop=True)
                    last.then_inc(prep_product, 1)
                    pe.wait_ge(w2_made, 1)
                    pe.wait_ge(b1_made, 1)
            with pe.Fori(FULL[0], FULL[-1] + 1) as t:
                turn(t)
            for t in range(FULL[-1] + 1, TURNS):
                turn(t)

        @block.scalar
        def _(act):
            def copy_out(t, name, dst, freed_t, freed):
                act.wait_ge(product.sem, product.after(t, name))
                act.wait_ge(product.sem, product.after(freed_t, freed))
                nc.scalar.activation(dst, bank(name)[:], ACT.Copy).then_inc(drained[BANK[name]].sem, 1)

            def gelus(t, s):
                for c in range(CH):
                    name = f"{s}.up{c}"
                    act.wait_ge(product.sem, product.after(t, name))
                    if c == 0:
                        act.wait_ge(product.sem, product.after(t - 1, f"{s}.down"))
                    nc.scalar.activation(hid[s][:, c], bank(name)[:], ACT.Gelu, bias=b1[:, c:c + 1]
                                         ).then_inc(drained[BANK[name]].sem, 1)

            def exponentials(t, j):
                act.wait_ge(drained["S"].sem, drained["S"].after(t, f"W.S{j}"))
                p = probs[:, j % 2].rearrange("p h k u -> p (h k u)")
                nc.scalar.activation(p, p, ACT.Exp).then_inc(probs_ready.sem, 1)

            def probs_out(t, j):
                name = f"W.T{j}"
                act.wait_ge(product.sem, product.after(t, name))
                act.wait_ge(product.sem, product.after(t if j >= 2 else t - 1, f"W.PV{(j - 2) % 4}"))
                nc.scalar.activation(probs_t[:, j % 2], ps_t[:], ACT.Copy).then_inc(drained["T"].sem, 1)

            def phi_parts(t, name, src, neg, e):
                nc.scalar.activation(neg, src, ACT.Relu, scale=-1.0).then_inc(negated.sem, 1)
                act.wait_ge(negated.sem, negated.after(t, name))
                nc.scalar.activation(e, neg, ACT.Exp, scale=-1.0).then_inc(phi_exp.sem, 1)

            def linear_parts(t):
                act.wait_ge(product.sem, product.after(t, "L.q"))
                act.wait_ge(product.sem, product.after(t - 1, "L.out1"))
                phi_parts(t, "L.q", bank("L.q")[:], neg_q[:], phi_q[:])
                for m in range(2):
                    name = f"L.k{m}"
                    kv = bank(name)[:].rearrange("p (j n) -> p j n", j=2)
                    act.wait_ge(product.sem, product.after(t, name))
                    if m == 0:
                        act.wait_ge(product.sem, product.after(t - 1, "L.kv"))
                        act.wait_ge(cleared, N_CLEARED)
                    nc.scalar.activation(v_ext[:, 2 * m:2 * m + 2, 0:DIM], kv[:, :, P:2 * P], ACT.Copy)
                    phi_parts(t, name, kv[:, :, 0:P], neg_k[:, m], phi_k[:, 2 * m:2 * m + 2])

            def attention_inputs_out(t):
                act.wait_ge(product.sem, product.after(t, "P.kv"))
                act.wait_ge(kx_in.sem, kx_in.after(t - 1, "P.kx"))
                act.wait_ge(v_in.sem, v_in.after(t - 1, "P.v"))
                act.wait_ge(cleared, N_CLEARED)
                for i, (to, first) in enumerate(((PAD, 0), (0, P - PAD))):
                    last = nc.scalar.activation(
                        kv_t[:].rearrange("p (b i) n -> p b i n", i=TPB)[:, :, i, to:to + P + PAD],
                        bank("P.kv")[0:2 * KV * HD].rearrange("p (b n) -> p b n", b=GB)[:, :, first:first + P + PAD],
                        ACT.Identity, bias=bkv_s[:])
                last.then_inc(drained[BANK["P.kv"]].sem, 1)
                act.wait_ge(product.sem, product.after(t, "P.q"))
                act.wait_ge(product.sem, product.after(t, "W.S3"))
                nc.scalar.activation(q_t[:], bank("P.q")[:], ACT.Identity, bias=bq_s[:]
                                     ).then_inc(drained[BANK["P.q"]].sem, 1)

            def turn(t):
                w, f, l, g, p = (active(t, s) for s in "WFLGP")
                if l:
                    copy_out(t, "L.xT", x_t["L"][:], t - 1, "L.k1")
                    linear_parts(t)
                if w:
                    exponentials(t, 0)
                    probs_out(t, 0)
                    exponentials(t, 1)
                    probs_out(t, 1)
                    exponentials(t, 2)
                    probs_out(t, 2)
                if f:
                    copy_out(t, "F.xT", x_t["F"][:], t - 1, f"F.up{CH - 1}")
                if w:
                    exponentials(t, 3)
                if f:
                    if isinstance(t, int) and t == LAG["F"]:
                        act.wait_ge(b1_made, 1)
                    gelus(t, "F")
                if p:
                    copy_out(t, "P.xT", x_t["P"][:], t - 1, "P.q")
                    attention_inputs_out(t)
                if w:
                    probs_out(t, 3)
                if g:
                    copy_out(t, "G.xT", x_t["G"][:], t - 1, f"G.up{CH - 1}")
                    gelus(t, "G")
                if w:
                    copy_out(t, "W.oT", o_wt[:], t - 1, "W.proj")
                if l:
                    copy_out(t, "L.oT", o_lt[:], t - 1, "L.proj")

            act.wait_ge(weights_in, 16 * N_WEIGHTS)
            for t in range(FULL[0]):
                turn(t)
            with act.Fori(FULL[0], FULL[-1] + 1) as t:
                turn(t)
            for t in range(FULL[-1] + 1, TURNS):
                turn(t)

        @block.vector
        def _(dve):
            def moments(t, s):
                for j in range(TILES):
                    last = nc.vector.bn_stats(stats[s][:, j], xs[s][:, j])
                last.then_inc(vec.sem, 1)
                seen, read = value(dve, vec.after(t, f"{s}.bn")), value(dve, normed.after(t - 1, f"{s}.xn"))
                dve.wait_ge(consts_in, 16 * 4)
                dve.wait_ge(vec.sem, seen)
                dve.wait_ge(normed.sem, read)
                for j in range(TILES):
                    last = nc.vector.bn_aggr(mv[s][:, j], stats[s][:, j])
                last.then_inc(vec.sem, 1)

            def residual(t, s, name, base, summed):
                dve.wait_ge(product.sem, product.after(t, name))
                dve.wait_ge(biased.sem, biased.after(t - 1, f"{summed}.xb"))
                own = drained[BANK[name]]
                nc.vector.tensor_tensor(xs[s][:].rearrange("p j n -> p (j n)"), bank(name)[:],
                                        xb[base][:].rearrange("p j n -> p (j n)"), ALU.add).then_inc(own.sem, 1)
                if s != "G":
                    dve.wait_ge(own.sem, own.after(t, name))
                    moments(t, s)

            def shift_by_max(t, j):
                dve.wait_ge(product.sem, product.after(t, f"W.S{j}"))
                s = ps_s[:].rearrange("p a (h u) -> p (a h) u", u=SPAN)
                nc.vector.tensor_reduce(rowmax[:, j], s, AX_X, ALU.max).then_inc(vec.sem, 1)
                dve.wait_ge(vec.sem, vec.after(t, f"W.max{j}"))
                dve.wait_ge(product.sem, product.after(t if j >= 2 else t - 1, f"W.T{(j - 2) % 4}"))
                m = rowmax[:, j].rearrange("p (k h a) -> p k h a", k=KV, a=1).to_broadcast([P, KV, HPK, SPAN])
                nc.vector.tensor_tensor(probs[:, j % 2].rearrange("p h k u -> p k h u"),
                                        ps_s[:].rearrange("p k (h u) -> p k h u", u=SPAN), m, ALU.subtract
                                        ).then_inc(drained["S"].sem, 1)

            def head_outputs(t, j):
                name = f"W.PV{j}"
                own = drained[BANK[name]]
                dve.wait_ge(product.sem, product.after(t, name))
                nc.vector.transpose(o_raw[:, j % 2].rearrange("p h r -> p (h r)"), bank(name)[:, 0:HPK * 32]
                                    ).then_inc(own.sem, 1)
                dve.wait_ge(own.sem, own.after(t, name))
                nc.vector.reciprocal(recip[:, j % 2], o_raw[:, j % 2, :, KV * HD:KV * HD + KV]
                                     .rearrange("p h k -> p k h")).then_inc(vec.sem, 1)
                dve.wait_ge(vec.sem, vec.after(t, f"W.rs{j}"))
                if j == 0:
                    dve.wait_ge(product.sem, product.after(t - 1, "W.oT"))
                nc.vector.tensor_tensor(
                    o_w[:, j].rearrange("p (k h d) -> p k h d", k=KV, d=HD),
                    o_raw[:, j % 2, :, 0:KV * HD].rearrange("p h (k d) -> p k h d", k=KV),
                    recip[:, j % 2].rearrange("p k (h a) -> p k h a", a=1).to_broadcast([P, KV, HPK, HD]),
                    ALU.mult).then_inc(vec.sem, 1)

            def phi(t, name, src, out_):
                dve.wait_ge(phi_exp.sem, phi_exp.after(t, name))
                nc.vector.scalar_tensor_tensor(out_, src, 0.0, out_, ALU.max, ALU.add
                                               ).then_inc(drained[BANK[name]].sem, 1)

            def linear_normalised(t, m):
                name = f"L.out{m}"
                src = bank(name)[:, 0:2 * KVW].rearrange("p (j n) -> p j n", j=2)
                dve.wait_ge(product.sem, product.after(t, name))
                nc.vector.tensor_scalar(norm[:, m], src[:, :, DIM:KVW], LIN_EPS, None, ALU.add
                                        ).then_inc(vec.sem, 1)
                dve.wait_ge(vec.sem, vec.after(t, f"L.nrm{m}"))
                nc.vector.reciprocal(rnorm[:, m], norm[:, m]).then_inc(vec.sem, 1)
                dve.wait_ge(vec.sem, vec.after(t, f"L.rn{m}"))
                if m == 0:
                    dve.wait_ge(product.sem, product.after(t - 1, "L.oT"))
                nc.vector.tensor_tensor(
                    o_l[:, 2 * m:2 * m + 2].rearrange("p j (h d) -> p j h d", d=HD),
                    src[:, :, 0:DIM].rearrange("p j (h d) -> p j h d", d=HD),
                    rnorm[:, m].rearrange("p j (h a) -> p j h a", a=1).to_broadcast([P, 2, HEADS, HD]),
                    ALU.mult).then_inc(drained[BANK[name]].sem, 1)

            def butterfly_up():
                src, dst = w1, w1b
                rsrc, rdst = b1row, b1rowb
                for s in range(STAGES):
                    dve.wait_ge(up_in[s], 16)
                    dve.wait_ge(up_step, 3 * s)
                    products(nc.vector, up_s[:, s % SLOTS], s, src, prod0, prod1, up_step)
                    dve.wait_ge(bias_step, 3 * s)
                    products(nc.vector, up_s[:, s % SLOTS], s, rsrc, row0, row1, bias_step, rows=1)
                    dve.wait_ge(up_step, 3 * s + 2)
                    nc.vector.tensor_tensor(paired(dst, s), split(prod0, s), split(prod1, s), ALU.add
                                            ).then_inc(up_step, 1)
                    dve.wait_ge(bias_step, 3 * s + 2)
                    nc.vector.tensor_tensor(paired(rdst, s, 1), split(row0, s, 1), split(row1, s, 1), ALU.add
                                            ).then_inc(bias_step, 1)
                    src, dst = dst, src
                    rsrc, rdst = rdst, rsrc
                assert src is w1b
                dve.wait_ge(bias_step, 3 * STAGES)
                nc.vector.tensor_tensor(b1rowb[:], b1rowb[:], upb_row[:], ALU.add).then_inc(bias_step, 1)

            def values_out(t):
                own = drained[BANK["W.V"]]
                dve.wait_ge(product.sem, product.after(t, "W.V"))
                dve.wait_ge(product.sem, product.after(t - 1, "W.PV3"))
                nc.vector.tensor_copy(vx[:].rearrange("p j c r -> p (j c r)"), bank("W.V")[:]
                                      ).then_inc(own.sem, 1)

            def linear_state_out(t):
                dve.wait_ge(product.sem, product.after(t, "L.kv"))
                dve.wait_ge(product.sem, product.after(t - 1, "L.out1"))
                nc.vector.tensor_tensor(
                    kvs[:], bank("L.kv")[:, 0:GB * KVW].rearrange("p (b n) -> p b n", b=GB),
                    kvmask[:].rearrange("p (a n) -> p a n", a=1).to_broadcast([P, GB, KVW]), ALU.mult
                ).then_inc(drained[BANK["L.kv"]].sem, 1)

            def turn(t):
                w, f, l, g, p = (active(t, s) for s in "WFLGP")
                if w:
                    shift_by_max(t, 0)
                if l:
                    phi(t, "L.q", bank("L.q")[:], phi_q[:])
                    for m in range(2):
                        phi(t, f"L.k{m}", bank(f"L.k{m}")[:].rearrange("p (j n) -> p j n", j=2)[:, :, 0:P],
                            phi_k[:, 2 * m:2 * m + 2])
                if p:
                    dve.wait_ge(x_in.sem, x_in.after(t, "P.x"))
                    moments(t, "P")
                if w:
                    shift_by_max(t, 1)
                if l:
                    linear_state_out(t)
                if w:
                    values_out(t)
                    shift_by_max(t, 2)
                    head_outputs(t, 0)
                if l:
                    linear_normalised(t, 0)
                    linear_normalised(t, 1)
                if w:
                    shift_by_max(t, 3)
                    head_outputs(t, 1)
                    head_outputs(t, 2)
                    head_outputs(t, 3)
                if f:
                    residual(t, "F", "F.down", "W", "W")
                if w:
                    residual(t, "W", "W.proj", "P", "W")
                if l:
                    residual(t, "L", "L.proj", "F", "L")
                if g:
                    dve.wait_ge(y_out.sem, y_out.after(t - 1, "G.y"))
                    residual(t, "G", "G.down", "L", "L")

            dve.wait_ge(consts_in, 16 * 4)
            nc.vector.tensor_copy(identb[:], ident[:]).then_inc(consts_made, 1)
            nc.vector.tensor_copy(bandb[:], band[:].rearrange("p (a u) -> p a u", a=1)
                                  .to_broadcast([P, HPK, SPAN])).then_inc(consts_made, 1)
            for t in range(FULL[0]):
                turn(t)
                if t == 0:
                    dve.wait_ge(weights_in, 16 * N_WEIGHTS)
                    butterfly_up()
                    dve.wait_ge(prep_product, 2)
                    nc.vector.tensor_copy(w2[:], ps_t[:, 0:CH]).then_inc(w2_made, 1)
                    nc.vector.tensor_copy(b1[:], ps_t[:, CH, 0:CH]).then_inc(b1_made, 1)
            with dve.Fori(FULL[0], FULL[-1] + 1) as t:
                turn(t)
            for t in range(FULL[-1] + 1, TURNS):
                turn(t)


N_WEIGHTS = 17
N_CLEARED = 3


def constants():
    ident = np.eye(P, dtype=np.float32)
    row, col = np.arange(P)[:, None], np.arange(P)[None, :]
    same = (row // HD == col // HD).astype(np.float32)
    of_head = (row // HD == np.arange(HEADS)[None, :]).astype(np.float32)
    kvmask = np.concatenate([same, of_head], axis=1)
    t, u = np.arange(P)[:, None] % WIN, np.arange(SPAN)[None, :]
    band = np.where((u >= t) & (u < t + WIN), 0.0, MASKED).astype(np.float32)
    vones = np.zeros((P, KV * SPAN), np.float32)
    for c in range(4):
        for kv in range(KV):
            vones[32 * c + KV * HD + kv, kv * SPAN:(kv + 1) * SPAN] = 1.0
    return ident, kvmask, band, vones


_W = "L0_attn_a_"
_B = "L0_attn_b_"
_F = "L0_ffn_"


def kernel(**inputs):
    import concourse.bacc as _bacc
    from concourse.bass_utils import run_bass_kernel_spmd as _run

    a = {k: np.asarray(v) for k, v in inputs.items()}
    ident, kvmask, band, vones = constants()
    up = np.ascontiguousarray(a[_F + "up_weights"].transpose(0, 2, 3, 1)).reshape(STAGES, 2 * HID)
    down = np.ascontiguousarray(a[_F + "down_weights"].transpose(0, 3, 2, 1)).reshape(STAGES, 2 * HID)
    arrays = {
        "x": a[_W + "x"], "wq": a[_W + "Wq"], "bq": a[_W + "bq"], "wk": a[_W + "Wk"], "bk": a[_W + "bk"],
        "wv": a[_W + "Wv"], "bv": a[_W + "bv"], "wo": a[_W + "Wo"], "bo": a[_W + "bo"],
        "wqkv_t": a[_B + "Wqkv"].T, "wproj_t": a[_B + "Wproj"].T, "bproj": a[_B + "bproj"],
        "w_exp": a[_F + "W_exp"], "b_exp": a[_F + "b_exp"], "up_w": up, "up_b": a[_F + "up_bias"],
        "down_w": down, "w_con_t": a[_F + "W_con"].T, "b_con": a[_F + "b_con"], "down_b": a[_F + "down_bias"],
        "ident_c": ident, "kvmask_c": kvmask, "band_c": band, "vones_c": vones,
    }
    arrays = {f"in_{k}": np.ascontiguousarray(v) for k, v in arrays.items()}
    nc = _bacc.Bacc("TRN2", target_bir_lowering=False, num_devices=1)
    args = [nc.dram_tensor(k, v.shape, mybir.dt.from_np(v.dtype), kind="ExternalInput").ap()
            for k, v in arrays.items()]
    args.append(nc.dram_tensor("out_x", (BATCH, SEQ, DIM), F32, kind="ExternalOutput").ap())
    window_and_linear_attention_with_butterfly_ffn(nc, *args)
    r = _run(nc, [arrays], core_ids=[0])
    return r.results[0]["out_x"]
```
